# Optimizing a Trainium2 kernel written in Bass

```python
import numpy as np
import jax
import jax.numpy as jnp

def _softmax(x, axis=-1):
    return jax.nn.softmax(x, axis=axis)

def _gelu(x):
    return jax.nn.gelu(x, approximate=True)

def _silu(x):
    return jax.nn.silu(x)

def _sigmoid(x):
    return jax.nn.sigmoid(x)

def _layernorm(x, axis=-1, eps=1e-05):
    m = jnp.mean(x, axis=axis, keepdims=True)
    v = jnp.var(x, axis=axis, keepdims=True)
    return (x - m) / jnp.sqrt(v + eps)

def _scatter_add(tgt, idx, src, axis=0):
    return tgt.at[idx].add(src)

def _segment_sum(src, seg, n):
    return jax.ops.segment_sum(src, seg, n)
kernel_name = 'mk_rec_standalone_d1_rec_r8_48ca29'

def setup_inputs(seed: int=0):
    np.random.seed(seed)
    _w = jnp.asarray

    def _rec_inputs():
        import jax
        import jax.numpy as jnp
        _rk = jax.random.key(seed)
        r_inputs = 0.000470451 + 0.999764 * jax.random.normal(jax.random.fold_in(_rk, 1), (2048, 32, 64), jnp.float32)
        return r_inputs
    r_inputs = _rec_inputs()

    def _L0_rec_setup():
        import jax, jax.numpy as jnp
        import numpy as np
        NUM_FIELDS = 32
        EMB_DIM = 64
        BATCH = 1024
        key = jax.random.key(seed)
        inputs = jax.random.normal(key, (BATCH, NUM_FIELDS, EMB_DIM), dtype=jnp.float32)
        return {'inputs': inputs}
    _L0_rec_all = _L0_rec_setup()
    _L0_rec_in = {k: v for k, v in _L0_rec_all.items() if k in ()}
    del _L0_rec_all
    return {'r_inputs': r_inputs}

def reference(r_inputs):
    import jax
    import jax.numpy as jnp

    def _L0_rec_ref(inputs):
        import jax, jax.numpy as jnp
        import numpy as np
        NUM_FIELDS = 32
        EMB_DIM = 64
        BATCH = 1024
        F, D = (NUM_FIELDS, EMB_DIM)
        x = inputs.reshape(-1, F, D)
        B = x.shape[0]
        xt = jnp.transpose(x, (0, 2, 1))
        had = jnp.einsum('bhd,bmd->bhmd', xt, xt)
        had = had.reshape(B, F, D, D)
        iu, ju = jnp.triu_indices(D, k=1)
        V = had[:, :, iu, ju]
        return V.reshape(B, -1)
    y = _L0_rec_ref(r_inputs)
    return y

_drawn_inputs = setup_inputs


def setup_inputs(seed=0):
    import zlib

    import numpy as np

    out = dict(_drawn_inputs(seed))
    spreads = {}
    factors = {}
    for name, (base, spread) in spreads.items():
        noise = np.random.default_rng([zlib.crc32(name.encode()), seed]).standard_normal(out[name].shape)
        drawn = base * np.exp(spread * noise) if base else spread * noise
        out[name] = jnp.asarray(drawn.astype(out[name].dtype))
    for name, factor in factors.items():
        out[name] = (out[name] * factor).astype(out[name].dtype)
    return out
```

```python
from contextlib import ExitStack

import concourse.bass as bass
from concourse import mybir

F32 = mybir.dt.float32
MULT = mybir.AluOpType.mult

P = 128
SLOTS = 3
BUFFERS = 3
CHUNKS = 5
FIRST_SHARES = (1, 2, 3, 4, 5, 5, 5, 5)
FIRST_CHUNKS = len(FIRST_SHARES)


def cut_rows(row_starts, shares):
    rows, pairs, whole = len(row_starts) - 1, row_starts[-1], sum(shares)
    cuts, target = [0], 0
    for share in shares[:-1]:
        target += share * pairs / whole
        nearest = min(range(rows + 1), key=lambda r: abs(row_starts[r] - target))
        cuts.append(max(nearest, cuts[-1] + 1))
    cuts.append(rows)
    return list(zip(cuts[:-1], cuts[1:]))


def build(nc: bass.Bass, x_dram: bass.AP, out_dram: bass.AP):
    batch, D, H = x_dram.shape
    F = H // 2
    ROWS = H - 1
    row_starts = [i * (H - 1) - i * (i - 1) // 2 for i in range(ROWS + 1)]
    PAIRS = row_starts[-1]
    TILES = batch // P
    LOOPS = (TILES - 1) // SLOTS
    assert 1 + LOOPS * SLOTS == TILES and F == D and out_dram.shape[1] == F * PAIRS

    first_plan = cut_rows(row_starts, FIRST_SHARES)
    plan = cut_rows(row_starts, (1,) * CHUNKS)
    width = max(row_starts[r1] - row_starts[r0] for r0, r1 in plan + first_plan)

    x_tiles = x_dram.rearrange("(t p) d h -> t p (d h)", p=P)
    out_tiles = out_dram.rearrange("(t p) (f n) -> t p f n", p=P, f=F)

    LOOP_CHUNKS = SLOTS * CHUNKS
    assert LOOP_CHUNKS % BUFFERS == 0

    with ExitStack() as ctx:
        x_row = ctx.enter_context(nc.sbuf_tensor("x_row", [P, D * H], F32))
        expanded = ctx.enter_context(nc.sbuf_tensor("expanded", [P, SLOTS, F, 3 * D], F32))
        products = [ctx.enter_context(nc.sbuf_tensor(f"products{b}", [P, F, width], F32))
                    for b in range(BUFFERS)]
        x_loaded = ctx.enter_context(nc.semaphore("x_loaded"))
        tile_expanded = ctx.enter_context(nc.semaphore("tile_expanded"))
        chunk_computed = ctx.enter_context(nc.semaphore("chunk_computed"))
        chunk_stored = [ctx.enter_context(nc.semaphore(f"chunk_stored{b}"))
                        for b in range(BUFFERS)]
        block = ctx.enter_context(nc.Block())

        @block.scalar
        def _(act):
            def expand(t, slot, free_after):
                if not (isinstance(t, int) and t == 0):
                    act.wait_ge(tile_expanded, 2 * t)
                act.dma_start(x_row[:, :], x_tiles[t]).then_inc(x_loaded, 16)
                act.wait_ge(x_loaded, 16 * t + 16)
                if free_after is not None:
                    act.wait_ge(chunk_computed, free_after)
                by_field = x_row[:, :].rearrange("p (d f two) -> p f two d", d=D, two=2)
                even, odd = by_field[:, :, 0, :], by_field[:, :, 1, :]
                nc.scalar.copy(expanded[:, slot, :, 0:2 * D].rearrange("p f (c d) -> p f c d", c=2),
                               even.unsqueeze(2).broadcast_to([P, F, 2, D])).then_inc(tile_expanded, 1)
                nc.scalar.copy(expanded[:, slot, :, 2 * D:3 * D], odd).then_inc(tile_expanded, 1)

            for t in range(1 + SLOTS):
                expand(t, t % SLOTS, FIRST_CHUNKS if t == SLOTS else None)
            with act.Fori(1, LOOPS) as it:
                for u in range(SLOTS):
                    expand(1 + u + it * SLOTS, (1 + u) % SLOTS,
                           FIRST_CHUNKS + (1 + u - SLOTS) * CHUNKS + it * LOOP_CHUNKS)

        @block.vector
        def _(dve):
            def multiply(slot, rows, buffer):
                base = row_starts[rows[0]]
                for i in range(*rows):
                    place = products[buffer][:, :, row_starts[i] - base:row_starts[i + 1] - base]
                    if i < D:
                        first = expanded[:, slot, :, i + 1:2 * D]
                        second = expanded[:, slot, i, D + i + 1:3 * D]
                    else:
                        first = expanded[:, slot, :, D + i + 1:3 * D]
                        second = expanded[:, slot, i - D, D + i + 1:3 * D]
                    n = row_starts[i + 1] - row_starts[i]
                    last = nc.vector.tensor_tensor(place, first,
                                                   second.unsqueeze(1).broadcast_to([P, F, n]), MULT)
                return last

            dve.wait_ge(tile_expanded, 2)
            for c, rows in enumerate(first_plan):
                if c >= BUFFERS:
                    dve.wait_ge(chunk_stored[c % BUFFERS], 16 * (c // BUFFERS))
                multiply(0, rows, c % BUFFERS).then_inc(chunk_computed, 1)
            with dve.Fori(0, LOOPS) as it:
                for u in range(SLOTS):
                    dve.wait_ge(tile_expanded, 2 * (2 + u) + it * (2 * SLOTS))
                    for n, rows in enumerate(plan):
                        c = FIRST_CHUNKS + u * CHUNKS + n
                        dve.wait_ge(chunk_stored[c % BUFFERS],
                                    16 * (c // BUFFERS) + it * (16 * LOOP_CHUNKS // BUFFERS))
                        multiply((1 + u) % SLOTS, rows, c % BUFFERS).then_inc(chunk_computed, 1)

        @block.sync
        def _(sp):
            def store(t, rows, buffer):
                lo, hi = row_starts[rows[0]], row_starts[rows[1]]
                sp.dma_start(out_tiles[t][:, :, lo:hi],
                             products[buffer][:, :, 0:hi - lo]).then_inc(chunk_stored[buffer], 16)

            for c, rows in enumerate(first_plan):
                sp.wait_ge(chunk_computed, c + 1)
                store(0, rows, c % BUFFERS)
            with sp.Fori(0, LOOPS) as it:
                for u in range(SLOTS):
                    for n, rows in enumerate(plan):
                        c = FIRST_CHUNKS + u * CHUNKS + n
                        sp.wait_ge(chunk_computed, c + 1 + it * LOOP_CHUNKS)
                        store(1 + u + it * SLOTS, rows, c % BUFFERS)
            total = FIRST_CHUNKS + LOOPS * LOOP_CHUNKS
            for b in range(BUFFERS):
                sp.wait_ge(chunk_stored[b], 16 * len(range(b, total, BUFFERS)))


def kernel(r_inputs):
    import numpy as np
    import concourse.bacc as bacc
    from concourse.bass_utils import run_bass_kernel_spmd

    x = np.ascontiguousarray(r_inputs)
    batch, fields, dim = x.shape
    nc = bacc.Bacc("TRN2", target_bir_lowering=False, num_devices=1)
    x_dram = nc.dram_tensor("x_dram", x.shape, mybir.dt.from_np(x.dtype), kind="ExternalInput").ap()
    out_dram = nc.dram_tensor("out_dram", (batch, fields * dim * (dim - 1) // 2), F32,
                              kind="ExternalOutput").ap()
    build(nc, x_dram, out_dram)
    result = run_bass_kernel_spmd(nc, [{"x_dram": x}], core_ids=[0])
    return result.results[0]["out_dram"]
```

```python
from contextlib import ExitStack

import concourse.bass as bass
from concourse import mybir

F32 = mybir.dt.float32
MULT = mybir.AluOpType.mult

P = 128
SLOTS = 3
BUFFERS = 3
HALVES = 2


def triangle_chunks(H):
    D, half = H // 2, H // 4
    low, high = (0, half), (half, D)
    wide, middle, last = D // 2 - 2, D + 3, H - 1
    plan = [(0, wide, *low), (0, wide, *high), (wide, middle, *low), (wide, middle, *high),
            (middle, last, 0, D)]
    first_plan = [(0, 3, *low), (3, 7, *low), (0, 3, *high), (3, 7, *high),
                  (7, wide, *low), (7, wide, *high)] + plan[2:]
    return plan, first_plan


def build(nc: bass.Bass, x_dram: bass.AP, out_dram: bass.AP):
    batch, D, H = x_dram.shape
    F = H // 2
    ROWS = H - 1
    row_starts = [i * (H - 1) - i * (i - 1) // 2 for i in range(ROWS + 1)]
    PAIRS = row_starts[-1]
    TILES = batch // P
    LOOPS = (TILES - 1) // SLOTS
    assert 1 + LOOPS * SLOTS == TILES and F == D and out_dram.shape[1] == F * PAIRS

    plan, first_plan = triangle_chunks(H)
    CHUNKS, FIRST_CHUNKS = len(plan), len(first_plan)

    def pitch(chunk):
        return -(-(row_starts[chunk[1]] - row_starts[chunk[0]]) // 8) * 8

    buffer_size = max(pitch(chunk) * (chunk[3] - chunk[2]) for chunk in plan + first_plan)

    x_tiles = x_dram.rearrange("(t p) d h -> t p (d h)", p=P)
    out_tiles = out_dram.rearrange("(t p) (f n) -> t p f n", p=P, f=F)

    LOOP_CHUNKS = SLOTS * CHUNKS
    COPIES = 2 * HALVES
    assert LOOP_CHUNKS % BUFFERS == 0

    with ExitStack() as ctx:
        x_row = ctx.enter_context(nc.sbuf_tensor("x_row", [P, D * H], F32))
        expanded = ctx.enter_context(nc.sbuf_tensor("expanded", [P, SLOTS, F, 3 * D], F32))
        products = [ctx.enter_context(nc.sbuf_tensor(f"products{b}", [P, buffer_size], F32))
                    for b in range(BUFFERS)]

        def buffer_view(chunk, buffer):
            fields = chunk[3] - chunk[2]
            return products[buffer][:, 0:fields * pitch(chunk)].rearrange("p (f n) -> p f n", f=fields)

        x_loaded = ctx.enter_context(nc.semaphore("x_loaded"))
        tile_expanded = ctx.enter_context(nc.semaphore("tile_expanded"))
        chunk_computed = ctx.enter_context(nc.semaphore("chunk_computed"))
        chunk_stored = [ctx.enter_context(nc.semaphore(f"chunk_stored{b}"))
                        for b in range(BUFFERS)]
        block = ctx.enter_context(nc.Block())

        @block.scalar
        def _(act):
            def expand(t, slot, free_after):
                if not (isinstance(t, int) and t == 0):
                    act.wait_ge(tile_expanded, COPIES * t)
                act.dma_start(x_row[:, :], x_tiles[t]).then_inc(x_loaded, 16)
                act.wait_ge(x_loaded, 16 * t + 16)
                if free_after is not None:
                    act.wait_ge(chunk_computed, free_after)
                by_field = x_row[:, :].rearrange("p (d f two) -> p f two d", d=D, two=2)
                for half in range(HALVES):
                    f0, f1 = half * F // HALVES, (half + 1) * F // HALVES
                    even, odd = by_field[:, f0:f1, 0, :], by_field[:, f0:f1, 1, :]
                    twice = expanded[:, slot, f0:f1, 0:2 * D].rearrange("p f (c d) -> p f c d", c=2)
                    nc.scalar.copy(twice, even.unsqueeze(2).broadcast_to([P, f1 - f0, 2, D])
                                   ).then_inc(tile_expanded, 1)
                    nc.scalar.copy(expanded[:, slot, f0:f1, 2 * D:3 * D], odd).then_inc(tile_expanded, 1)

            for t in range(1 + SLOTS):
                expand(t, t % SLOTS, FIRST_CHUNKS if t == SLOTS else None)
            with act.Fori(1, LOOPS) as it:
                for u in range(SLOTS):
                    expand(1 + u + it * SLOTS, (1 + u) % SLOTS,
                           FIRST_CHUNKS + (1 + u - SLOTS) * CHUNKS + it * LOOP_CHUNKS)

        @block.vector
        def _(dve):
            def multiply(slot, chunk, buffer):
                r0, r1, f0, f1 = chunk
                view = buffer_view(chunk, buffer)
                for i in range(r0, r1):
                    place = view[:, :, row_starts[i] - row_starts[r0]:row_starts[i + 1] - row_starts[r0]]
                    if i < D:
                        first = expanded[:, slot, f0:f1, i + 1:2 * D]
                        second = expanded[:, slot, i, D + i + 1:3 * D]
                    else:
                        first = expanded[:, slot, f0:f1, D + i + 1:3 * D]
                        second = expanded[:, slot, i - D, D + i + 1:3 * D]
                    n = row_starts[i + 1] - row_starts[i]
                    last = nc.vector.tensor_tensor(place, first,
                                                   second.unsqueeze(1).broadcast_to([P, f1 - f0, n]), MULT)
                return last

            for c, chunk in enumerate(first_plan):
                if c == 0:
                    dve.wait_ge(tile_expanded, 2)
                if c == first_plan.index((0, 3, F // 2, F)):
                    dve.wait_ge(tile_expanded, COPIES)
                if c >= BUFFERS:
                    dve.wait_ge(chunk_stored[c % BUFFERS], 16 * (c // BUFFERS))
                multiply(0, chunk, c % BUFFERS).then_inc(chunk_computed, 1)
            with dve.Fori(0, LOOPS) as it:
                for u in range(SLOTS):
                    dve.wait_ge(tile_expanded, COPIES * (2 + u) + it * (COPIES * SLOTS))
                    for n, chunk in enumerate(plan):
                        c = FIRST_CHUNKS + u * CHUNKS + n
                        dve.wait_ge(chunk_stored[c % BUFFERS],
                                    16 * (c // BUFFERS) + it * (16 * LOOP_CHUNKS // BUFFERS))
                        multiply((1 + u) % SLOTS, chunk, c % BUFFERS).then_inc(chunk_computed, 1)

        @block.sync
        def _(sp):
            def store(t, chunk, buffer):
                r0, r1, f0, f1 = chunk
                lo, hi = row_starts[r0], row_starts[r1]
                sp.dma_start(out_tiles[t][:, f0:f1, lo:hi],
                             buffer_view(chunk, buffer)[:, :, 0:hi - lo]).then_inc(chunk_stored[buffer], 16)

            for c, chunk in enumerate(first_plan):
                sp.wait_ge(chunk_computed, c + 1)
                store(0, chunk, c % BUFFERS)
            with sp.Fori(0, LOOPS) as it:
                for u in range(SLOTS):
                    for n, chunk in enumerate(plan):
                        c = FIRST_CHUNKS + u * CHUNKS + n
                        sp.wait_ge(chunk_computed, c + 1 + it * LOOP_CHUNKS)
                        store(1 + u + it * SLOTS, chunk, c % BUFFERS)
            total = FIRST_CHUNKS + LOOPS * LOOP_CHUNKS
            for b in range(BUFFERS):
                sp.wait_ge(chunk_stored[b], 16 * len(range(b, total, BUFFERS)))


def kernel(r_inputs):
    import numpy as np
    import concourse.bacc as bacc
    from concourse.bass_utils import run_bass_kernel_spmd

    x = np.ascontiguousarray(r_inputs)
    batch, fields, dim = x.shape
    nc = bacc.Bacc("TRN2", target_bir_lowering=False, num_devices=1)
    x_dram = nc.dram_tensor("x_dram", x.shape, mybir.dt.from_np(x.dtype), kind="ExternalInput").ap()
    out_dram = nc.dram_tensor("out_dram", (batch, fields * dim * (dim - 1) // 2), F32,
                              kind="ExternalOutput").ap()
    build(nc, x_dram, out_dram)
    result = run_bass_kernel_spmd(nc, [{"x_dram": x}], core_ids=[0])
    return result.results[0]["out_dram"]
```

```python
from contextlib import ExitStack

import concourse.bass as bass
from concourse import mybir

F32 = mybir.dt.float32
MULT = mybir.AluOpType.mult

P = 128
SLOTS = 3
BUFFERS = 3
HALVES = 2


def triangle_chunks(H):
    D, half = H // 2, H // 4
    low, high = (0, half), (half, D)
    wide, middle, last = D // 2 - 2, D + 3, H - 1
    plan = [(0, wide, *low), (0, wide, *high), (wide, middle, *low), (wide, middle, *high),
            (middle, last, 0, D)]
    first_plan = [(0, 3, 0, half // 2), (0, 3, half // 2, half), (0, 3, *high)]
    for r0, r1 in ((3, 7), (7, wide), (wide, wide + D // 4), (wide + D // 4, middle)):
        first_plan += [(r0, r1, *low), (r0, r1, *high)]
    first_plan.append(plan[-1])
    return plan, first_plan


def build(nc: bass.Bass, x_dram: bass.AP, out_dram: bass.AP):
    batch, D, H = x_dram.shape
    F = H // 2
    ROWS = H - 1
    row_starts = [i * (H - 1) - i * (i - 1) // 2 for i in range(ROWS + 1)]
    PAIRS = row_starts[-1]
    TILES = batch // P
    LOOPS = (TILES - 1) // SLOTS
    assert 1 + LOOPS * SLOTS == TILES and F == D and out_dram.shape[1] == F * PAIRS

    plan, first_plan = triangle_chunks(H)
    CHUNKS, FIRST_CHUNKS = len(plan), len(first_plan)

    def pitch(chunk):
        return -(-(row_starts[chunk[1]] - row_starts[chunk[0]]) // 8) * 8

    buffer_size = max(pitch(chunk) * (chunk[3] - chunk[2]) for chunk in plan + first_plan)

    x_tiles = x_dram.rearrange("(t p) d h -> t p (d h)", p=P)
    out_tiles = out_dram.rearrange("(t p) (f n) -> t p f n", p=P, f=F)

    LOOP_CHUNKS = SLOTS * CHUNKS
    COPIES = 2 * HALVES
    assert LOOP_CHUNKS % BUFFERS == 0

    with ExitStack() as ctx:
        x_row = ctx.enter_context(nc.sbuf_tensor("x_row", [P, D * H], F32))
        expanded = ctx.enter_context(nc.sbuf_tensor("expanded", [P, SLOTS, F, 3 * D], F32))
        products = [ctx.enter_context(nc.sbuf_tensor(f"products{b}", [P, buffer_size], F32))
                    for b in range(BUFFERS)]

        x_tile2 = ctx.enter_context(nc.sbuf_tensor("x_tile2", [P, D * H], F32))
        x_tile0 = products[BUFFERS - 1][:, 0:D * H]

        def buffer_view(chunk, buffer):
            fields = chunk[3] - chunk[2]
            return products[buffer][:, 0:fields * pitch(chunk)].rearrange("p (f n) -> p f n", f=fields)

        tile0_loaded = ctx.enter_context(nc.semaphore("tile0_loaded"))
        tile2_loaded = ctx.enter_context(nc.semaphore("tile2_loaded"))
        x_loaded = ctx.enter_context(nc.semaphore("x_loaded"))
        tile_expanded = ctx.enter_context(nc.semaphore("tile_expanded"))
        chunk_computed = ctx.enter_context(nc.semaphore("chunk_computed"))
        chunk_stored = [ctx.enter_context(nc.semaphore(f"chunk_stored{b}"))
                        for b in range(BUFFERS)]
        block = ctx.enter_context(nc.Block())

        @block.scalar
        def _(act):
            def load(t, x_row, loaded):
                act.dma_start(x_row, x_tiles[t]).then_inc(loaded, 16)

            def expand(x_row, slot):
                by_field = x_row.rearrange("p (d f two) -> p f two d", d=D, two=2)
                for half in range(HALVES):
                    f0, f1 = half * F // HALVES, (half + 1) * F // HALVES
                    even, odd = by_field[:, f0:f1, 0, :], by_field[:, f0:f1, 1, :]
                    twice = expanded[:, slot, f0:f1, 0:2 * D].rearrange("p f (c d) -> p f c d", c=2)
                    nc.scalar.copy(twice, even.unsqueeze(2).broadcast_to([P, f1 - f0, 2, D])
                                   ).then_inc(tile_expanded, 1)
                    nc.scalar.copy(expanded[:, slot, f0:f1, 2 * D:3 * D], odd).then_inc(tile_expanded, 1)

            def load_and_expand(t, slot, chunks_before):
                act.wait_ge(tile_expanded, COPIES * t)
                load(t, x_row[:, :], x_loaded)
                act.wait_ge(x_loaded, 16 * (t + 2 - SLOTS))
                act.wait_ge(chunk_computed, chunks_before)
                expand(x_row[:, :], slot)

            starts = [(x_tile0, tile0_loaded), (x_row[:, :], x_loaded), (x_tile2[:, :], tile2_loaded)]
            for t, (place, loaded) in enumerate(starts):
                load(t, place, loaded)
            for t, (place, loaded) in enumerate(starts):
                act.wait_ge(loaded, 16)
                expand(place, t)
            load_and_expand(SLOTS, 0, FIRST_CHUNKS)
            with act.Fori(1, LOOPS) as it:
                for u in range(SLOTS):
                    load_and_expand(1 + u + it * SLOTS, (1 + u) % SLOTS,
                                    FIRST_CHUNKS + (1 + u - SLOTS) * CHUNKS + it * LOOP_CHUNKS)

        @block.vector
        def _(dve):
            def multiply(slot, chunk, buffer):
                r0, r1, f0, f1 = chunk
                view = buffer_view(chunk, buffer)
                for i in range(r0, r1):
                    place = view[:, :, row_starts[i] - row_starts[r0]:row_starts[i + 1] - row_starts[r0]]
                    if i < D:
                        first = expanded[:, slot, f0:f1, i + 1:2 * D]
                        second = expanded[:, slot, i, D + i + 1:3 * D]
                    else:
                        first = expanded[:, slot, f0:f1, D + i + 1:3 * D]
                        second = expanded[:, slot, i - D, D + i + 1:3 * D]
                    n = row_starts[i + 1] - row_starts[i]
                    last = nc.vector.tensor_tensor(place, first,
                                                   second.unsqueeze(1).broadcast_to([P, f1 - f0, n]), MULT)
                return last

            assert first_plan.index((0, 3, F // 2, F)) <= BUFFERS - 1
            for c, chunk in enumerate(first_plan):
                if c == 0:
                    dve.wait_ge(tile_expanded, 2)
                if c == first_plan.index((0, 3, F // 2, F)):
                    dve.wait_ge(tile_expanded, COPIES)
                if c >= BUFFERS:
                    dve.wait_ge(chunk_stored[c % BUFFERS], 16 * (c // BUFFERS))
                multiply(0, chunk, c % BUFFERS).then_inc(chunk_computed, 1)
            with dve.Fori(0, LOOPS) as it:
                for u in range(SLOTS):
                    dve.wait_ge(tile_expanded, COPIES * (2 + u) + it * (COPIES * SLOTS))
                    for n, chunk in enumerate(plan):
                        c = FIRST_CHUNKS + u * CHUNKS + n
                        dve.wait_ge(chunk_stored[c % BUFFERS],
                                    16 * (c // BUFFERS) + it * (16 * LOOP_CHUNKS // BUFFERS))
                        multiply((1 + u) % SLOTS, chunk, c % BUFFERS).then_inc(chunk_computed, 1)

        @block.sync
        def _(sp):
            def store(t, chunk, buffer):
                r0, r1, f0, f1 = chunk
                lo, hi = row_starts[r0], row_starts[r1]
                sp.dma_start(out_tiles[t][:, f0:f1, lo:hi],
                             buffer_view(chunk, buffer)[:, :, 0:hi - lo]).then_inc(chunk_stored[buffer], 16)

            for c, chunk in enumerate(first_plan):
                sp.wait_ge(chunk_computed, c + 1)
                store(0, chunk, c % BUFFERS)
            with sp.Fori(0, LOOPS) as it:
                for u in range(SLOTS):
                    for n, chunk in enumerate(plan):
                        c = FIRST_CHUNKS + u * CHUNKS + n
                        sp.wait_ge(chunk_computed, c + 1 + it * LOOP_CHUNKS)
                        store(1 + u + it * SLOTS, chunk, c % BUFFERS)
            total = FIRST_CHUNKS + LOOPS * LOOP_CHUNKS
            for b in range(BUFFERS):
                sp.wait_ge(chunk_stored[b], 16 * len(range(b, total, BUFFERS)))


def kernel(r_inputs):
    import numpy as np
    import concourse.bacc as bacc
    from concourse.bass_utils import run_bass_kernel_spmd

    x = np.ascontiguousarray(r_inputs)
    batch, fields, dim = x.shape
    nc = bacc.Bacc("TRN2", target_bir_lowering=False, num_devices=1)
    x_dram = nc.dram_tensor("x_dram", x.shape, mybir.dt.from_np(x.dtype), kind="ExternalInput").ap()
    out_dram = nc.dram_tensor("out_dram", (batch, fields * dim * (dim - 1) // 2), F32,
                              kind="ExternalOutput").ap()
    build(nc, x_dram, out_dram)
    result = run_bass_kernel_spmd(nc, [{"x_dram": x}], core_ids=[0])
    return result.results[0]["out_dram"]
```
